# Optimizing a Trainium2 kernel written in Bass

```python
import numpy as np
import jax
import jax.numpy as jnp

def _softmax(x, axis=-1):
    return jax.nn.softmax(x, axis=axis)

def _gelu(x):
    return jax.nn.gelu(x, approximate=True)

def _silu(x):
    return jax.nn.silu(x)

def _sigmoid(x):
    return jax.nn.sigmoid(x)

def _layernorm(x, axis=-1, eps=1e-05):
    m = jnp.mean(x, axis=axis, keepdims=True)
    v = jnp.var(x, axis=axis, keepdims=True)
    return (x - m) / jnp.sqrt(v + eps)

def _scatter_add(tgt, idx, src, axis=0):
    return tgt.at[idx].add(src)

def _segment_sum(src, seg, n):
    return jax.ops.segment_sum(src, seg, n)
kernel_name = 'mk_gnn_resnorm_d2_gnn_r8_e48da5'

def setup_inputs(seed: int=0):
    np.random.seed(seed)
    _w = jnp.asarray

    def _rec_inputs():
        import jax
        import jax.numpy as jnp
        _gk = jax.random.key(seed)
        x = -0.000202 + 1 * jax.random.normal(jax.random.fold_in(_gk, 1), (6250, 128), jnp.float32)
        src = jax.random.randint(jax.random.fold_in(_gk, 2), (100000,), 0, 6250, jnp.int32)
        dst = jnp.minimum((6250 * jax.random.uniform(jax.random.fold_in(_gk, 3), (100000,)) ** 2.0).astype(jnp.int32), 49999)
        _o = jnp.argsort(dst, stable=True)
        src = src[_o]
        dst = dst[_o]
        return (x, src, dst)
    x, src, dst = _rec_inputs()

    def _L0_gnn_setup():
        import jax, jax.numpy as jnp
        import numpy as np
        N = 6250
        E = 100000
        D = 128
        H = 256
        L = 4

        def _ln(x, g, b):
            m = jnp.mean(x, axis=-1, keepdims=True)
            v = jnp.var(x, axis=-1, keepdims=True)
            return (x - m) / jnp.sqrt(v + 1e-05) * g + b
        key = jax.random.key(seed)
        ks = jax.random.split(key, 16)

        def w(k, shape, fan):
            return jax.random.normal(k, shape, jnp.float32) / np.float32(np.sqrt(fan))
        return {'x': jax.random.normal(ks[0], (N, D), jnp.float32), 't': jax.random.uniform(ks[1], (1,), jnp.float32), 'edge_index': jax.random.randint(ks[2], (2, E), 0, N, jnp.int32), 'time_w1': w(ks[3], (1, H), 1), 'time_b1': jnp.zeros((H,), jnp.float32), 'time_w2': w(ks[4], (H, H), H), 'time_b2': jnp.zeros((H,), jnp.float32), 'in_w': w(ks[5], (D, H), D), 'in_b': jnp.zeros((H,), jnp.float32), 'gcn_w': w(ks[6], (L, H, H), H), 'gcn_b': jnp.zeros((L, H), jnp.float32), 'res_w1': w(ks[7], (L, H, H), H), 'res_b1': jnp.zeros((L, H), jnp.float32), 'res_g1': jnp.ones((L, H), jnp.float32), 'res_be1': jnp.zeros((L, H), jnp.float32), 'res_w2': w(ks[8], (L, H, H), H), 'res_b2': jnp.zeros((L, H), jnp.float32), 'res_g2': jnp.ones((L, H), jnp.float32), 'res_be2': jnp.zeros((L, H), jnp.float32), 'out_w1': w(ks[9], (H, H), H), 'out_b1': jnp.zeros((H,), jnp.float32), 'out_w2': w(ks[10], (H, D), H), 'out_b2': jnp.zeros((D,), jnp.float32)}
    _L0_gnn_all = _L0_gnn_setup()
    _L0_gnn_in = {k: v for k, v in _L0_gnn_all.items() if k in ('t', 'time_w1', 'time_b1', 'time_w2', 'time_b2', 'in_w', 'in_b', 'gcn_w', 'gcn_b', 'res_w1', 'res_b1', 'res_g1', 'res_be1', 'res_w2', 'res_b2', 'res_g2', 'res_be2', 'out_w1', 'out_b1', 'out_w2', 'out_b2')}
    del _L0_gnn_all

    def _L1_gnn_setup():
        import jax, jax.numpy as jnp
        import numpy as np
        BN_EPS = 1e-05
        key = jax.random.key(seed)
        ks = jax.random.split(key, 4)
        N, E, D = (6250, 100000, 128)
        x = jax.random.normal(ks[0], (N, D), dtype=jnp.float32)
        edge_index = jax.random.randint(ks[1], (2, E), 0, N, dtype=jnp.int64)
        W_l = jax.random.normal(ks[2], (D, D), dtype=jnp.float32) * (1.0 / np.sqrt(D))
        W_r = jax.random.normal(ks[3], (D, D), dtype=jnp.float32) * (1.0 / np.sqrt(D))
        b = jnp.zeros((D,), dtype=jnp.float32)
        gamma = jnp.ones((D,), dtype=jnp.float32)
        beta = jnp.zeros((D,), dtype=jnp.float32)
        return {'x': x, 'edge_index': edge_index, 'W_l': W_l, 'W_r': W_r, 'b': b, 'gamma': gamma, 'beta': beta}
    _L1_gnn_all = _L1_gnn_setup()
    _L1_gnn_in = {k: v for k, v in _L1_gnn_all.items() if k in ('W_l', 'W_r', 'b', 'gamma', 'beta')}
    del _L1_gnn_all
    return {'x': x, 'src': src, 'dst': dst, 'L0_gnn_t': _L0_gnn_in['t'], 'L0_gnn_time_w1': _L0_gnn_in['time_w1'], 'L0_gnn_time_b1': _L0_gnn_in['time_b1'], 'L0_gnn_time_w2': _L0_gnn_in['time_w2'], 'L0_gnn_time_b2': _L0_gnn_in['time_b2'], 'L0_gnn_in_w': _L0_gnn_in['in_w'], 'L0_gnn_in_b': _L0_gnn_in['in_b'], 'L0_gnn_gcn_w': _L0_gnn_in['gcn_w'], 'L0_gnn_gcn_b': _L0_gnn_in['gcn_b'], 'L0_gnn_res_w1': _L0_gnn_in['res_w1'], 'L0_gnn_res_b1': _L0_gnn_in['res_b1'], 'L0_gnn_res_g1': _L0_gnn_in['res_g1'], 'L0_gnn_res_be1': _L0_gnn_in['res_be1'], 'L0_gnn_res_w2': _L0_gnn_in['res_w2'], 'L0_gnn_res_b2': _L0_gnn_in['res_b2'], 'L0_gnn_res_g2': _L0_gnn_in['res_g2'], 'L0_gnn_res_be2': _L0_gnn_in['res_be2'], 'L0_gnn_out_w1': _L0_gnn_in['out_w1'], 'L0_gnn_out_b1': _L0_gnn_in['out_b1'], 'L0_gnn_out_w2': _L0_gnn_in['out_w2'], 'L0_gnn_out_b2': _L0_gnn_in['out_b2'], 'L1_gnn_W_l': _L1_gnn_in['W_l'], 'L1_gnn_W_r': _L1_gnn_in['W_r'], 'L1_gnn_b': _L1_gnn_in['b'], 'L1_gnn_gamma': _L1_gnn_in['gamma'], 'L1_gnn_beta': _L1_gnn_in['beta']}

def reference(x, src, dst, L0_gnn_t, L0_gnn_time_w1, L0_gnn_time_b1, L0_gnn_time_w2, L0_gnn_time_b2, L0_gnn_in_w, L0_gnn_in_b, L0_gnn_gcn_w, L0_gnn_gcn_b, L0_gnn_res_w1, L0_gnn_res_b1, L0_gnn_res_g1, L0_gnn_res_be1, L0_gnn_res_w2, L0_gnn_res_b2, L0_gnn_res_g2, L0_gnn_res_be2, L0_gnn_out_w1, L0_gnn_out_b1, L0_gnn_out_w2, L0_gnn_out_b2, L1_gnn_W_l, L1_gnn_W_r, L1_gnn_b, L1_gnn_gamma, L1_gnn_beta):
    import jax
    import jax.numpy as jnp

    def _L0_gnn_ref(x, t, edge_index, time_w1, time_b1, time_w2, time_b2, in_w, in_b, gcn_w, gcn_b, res_w1, res_b1, res_g1, res_be1, res_w2, res_b2, res_g2, res_be2, out_w1, out_b1, out_w2, out_b2):
        import jax, jax.numpy as jnp
        import numpy as np
        N = 6250
        E = 100000
        D = 128
        H = 256
        L = 4

        def _ln(x, g, b):
            m = jnp.mean(x, axis=-1, keepdims=True)
            v = jnp.var(x, axis=-1, keepdims=True)
            return (x - m) / jnp.sqrt(v + 1e-05) * g + b
        silu = jax.nn.silu
        te = silu(t[:, None] @ time_w1 + time_b1) @ time_w2 + time_b2
        h = x @ in_w + in_b + te
        loops = jnp.arange(N, dtype=edge_index.dtype)
        src = jnp.concatenate([edge_index[0], loops])
        dst = jnp.concatenate([edge_index[1], loops])
        deg = jax.ops.segment_sum(jnp.ones_like(dst, jnp.float32), dst, num_segments=N)
        dinv = jnp.where(deg > 0, 1.0 / jnp.sqrt(deg), 0.0)
        norm = (dinv[src] * dinv[dst])[:, None]
        for i in range(L):
            xw = h @ gcn_w[i]
            agg = jax.ops.segment_sum(xw[src] * norm, dst, num_segments=N) + gcn_b[i]
            h = h + agg
            r = silu(_ln(h @ res_w1[i] + res_b1[i], res_g1[i], res_be1[i]))
            r = _ln(r @ res_w2[i] + res_b2[i], res_g2[i], res_be2[i])
            h = h + r
        return silu(h @ out_w1 + out_b1) @ out_w2 + out_b2

    def _L1_gnn_ref(x, edge_index, W_l, W_r, b, gamma, beta):
        import jax, jax.numpy as jnp
        import numpy as np
        BN_EPS = 1e-05
        N = x.shape[0]
        src, dst = (edge_index[0], edge_index[1])
        msgs = x[src]
        agg = jax.ops.segment_sum(msgs, dst, num_segments=N)
        cnt = jax.ops.segment_sum(jnp.ones((src.shape[0],), dtype=x.dtype), dst, num_segments=N)
        mean = agg / jnp.maximum(cnt, 1.0)[:, None]
        h = mean @ W_l.T + x @ W_r.T + b
        h = jax.nn.relu(h)
        mu = jnp.mean(h, axis=0)
        var = jnp.var(h, axis=0)
        h = (h - mu) * jax.lax.rsqrt(var + BN_EPS) * gamma + beta
        return x + h
    edge_index = jnp.stack([src, dst])
    x = _layernorm(x + _L0_gnn_ref(x, L0_gnn_t, edge_index, L0_gnn_time_w1, L0_gnn_time_b1, L0_gnn_time_w2, L0_gnn_time_b2, L0_gnn_in_w, L0_gnn_in_b, L0_gnn_gcn_w, L0_gnn_gcn_b, L0_gnn_res_w1, L0_gnn_res_b1, L0_gnn_res_g1, L0_gnn_res_be1, L0_gnn_res_w2, L0_gnn_res_b2, L0_gnn_res_g2, L0_gnn_res_be2, L0_gnn_out_w1, L0_gnn_out_b1, L0_gnn_out_w2, L0_gnn_out_b2), axis=-1)
    x = _layernorm(x + _L1_gnn_ref(x, edge_index, L1_gnn_W_l, L1_gnn_W_r, L1_gnn_b, L1_gnn_gamma, L1_gnn_beta), axis=-1)
    return x

_drawn_inputs = setup_inputs


def setup_inputs(seed=0):
    import zlib

    import numpy as np

    out = dict(_drawn_inputs(seed))
    spreads = {'L0_gnn_time_b1': (0.0, 0.1),
     'L0_gnn_time_b2': (0.0, 0.1),
     'L0_gnn_in_b': (0.0, 0.1),
     'L0_gnn_gcn_b': (0.0, 0.1),
     'L0_gnn_res_b1': (0.0, 0.1),
     'L0_gnn_res_g1': (1.0, 0.2),
     'L0_gnn_res_be1': (0.0, 0.1),
     'L0_gnn_res_b2': (0.0, 0.1),
     'L0_gnn_res_g2': (1.0, 0.2),
     'L0_gnn_res_be2': (0.0, 0.1),
     'L0_gnn_out_b1': (0.0, 0.1),
     'L0_gnn_out_b2': (0.0, 0.1),
     'L1_gnn_b': (0.0, 0.1),
     'L1_gnn_gamma': (1.0, 0.2),
     'L1_gnn_beta': (0.0, 0.1)}
    factors = {'L0_gnn_time_w1': 7.038}
    for name, (base, spread) in spreads.items():
        noise = np.random.default_rng([zlib.crc32(name.encode()), seed]).standard_normal(out[name].shape)
        drawn = base * np.exp(spread * noise) if base else spread * noise
        out[name] = jnp.asarray(drawn.astype(out[name].dtype))
    for name, factor in factors.items():
        out[name] = (out[name] * factor).astype(out[name].dtype)
    return out
```

```python
from contextlib import ExitStack

import concourse.bass as bass
from concourse import mybir

ALU = mybir.AluOpType
ACT = mybir.ActivationFunctionType
F32 = mybir.dt.float32
F32R = mybir.dt.float32r
BF16 = mybir.dt.bfloat16
F16 = mybir.dt.float16
I32 = mybir.dt.int32

P = 128
GROUP = 8
BATCH = 16
BANKS = 8
BANK = 512
EPS = 1e-5
PAD_DST = 1 << 20


def gnn_kernel(nc: bass.Bass, a: dict, out: bass.AP):
    N, D = a["x"].shape
    E = a["src"].shape[0]
    H = a["L0_gnn_in_w"].shape[1]
    L = a["L0_gnn_gcn_w"].shape[0]
    T = -(-N // P)
    NP = T * P
    KH = H // P
    NG = NP // GROUP
    CODES = T * GROUP
    ROWS = -(-E // P)
    CW = 112
    ROWS_PAD = -(-(ROWS + 1) // CW) * CW
    CK = ROWS_PAD // CW
    PAIRS = -(-(ROWS + NG) // CW) * CW
    PK = PAIRS // CW
    assert CW % BATCH == 0 and PAIRS % BATCH == 0 and PAIRS >= ROWS + NG and ROWS_PAD > ROWS and NG % CW == 0
    NV = NG + 1
    TAIL = ROWS_PAD * P - E
    GB = NG // CW
    XB = 7
    assert T % XB == 0
    PIECES = T // XB
    TG = P // GROUP
    LAST = N - (T - 1) * P

    def scratch(name, shape, dt):
        return nc.dram_tensor(name, shape, dt, kind="Internal").ap()

    src_rows = scratch("src_rows", (ROWS_PAD, P), I32)
    dst_rows = scratch("dst_rows", (ROWS_PAD, P), I32)
    pair_table = scratch("pair_table", (4, PAIRS), I32)
    in_degree = scratch("in_degree", (NP,), F32)
    counts = scratch("counts", (NG + BATCH, P, CODES), BF16)
    feats = scratch("feats", (NP, 2 * H), F32)
    h_rows = scratch("h_rows", (NP, H), F32)
    x1_rows = scratch("x1_rows", (NP, 2 * D), F32)

    ctx = ExitStack()
    with ctx:
        held = []

        def sem(name):
            held.append(nc.alloc_semaphore(name))
            return held[-1]

        def end_stage():
            nc.all_engine_barrier()
            nc.clear_and_free_semaphores(held)
            held.clear()
            nc.all_engine_barrier()

        ident = ctx.enter_context(nc.sbuf_tensor("ident", [P, P], F32))
        deg_inv_sqrt = ctx.enter_context(nc.sbuf_tensor("deg_inv_sqrt", [P, T], F32))
        deg_inv = ctx.enter_context(nc.sbuf_tensor("deg_inv", [P, T], F32))
        banks = ctx.enter_context(nc.psum_tensor("banks", [P, BANKS * BANK], F32))
        build_counts(nc, a, locals())
        end_stage()
        start_features(nc, a, locals())
        end_stage()
        gcn_layers(nc, a, locals())
        end_stage()
        output_mlp(nc, a, locals())
        end_stage()
        sage_layer(nc, a, locals())


def build_counts(nc, a, g):
    (N, E, T, NP, NG, CODES, ROWS, CW, ROWS_PAD, CK, PAIRS, PK, NV, TAIL, GB) = (
        g[k] for k in ("N", "E", "T", "NP", "NG", "CODES", "ROWS", "CW", "ROWS_PAD", "CK", "PAIRS", "PK",
                       "NV", "TAIL", "GB"))
    ident, banks, deg_inv_sqrt, deg_inv = g["ident"], g["banks"], g["deg_inv_sqrt"], g["deg_inv"]
    src_rows, dst_rows, pair_table, in_degree, counts = (
        g[k] for k in ("src_rows", "dst_rows", "pair_table", "in_degree", "counts"))
    with ExitStack() as ctx:
        def sb(name, shape, dt=F32):
            return ctx.enter_context(nc.sbuf_tensor(name, shape, dt))

        def sem(name):
            return g["sem"](name)

        tail_dst = sb("tail_dst", [1, TAIL], I32)
        tail_src = sb("tail_src", [1, TAIL], I32)
        ends_i = sb("ends_i", [CW, 2, CK, 1], I32)
        ends = sb("ends", [CW, 2, CK])
        bounds = sb("bounds", [P, NV])
        below = sb("below", [CW, 2 * CK, NV], BF16)
        ones_bf = sb("ones_bf", [P, P], BF16)
        zeros_bf = sb("zeros_bf", [P, 512], BF16)
        ones_row = sb("ones_row", [P, NG])
        first_row = sb("first_row", [P, NV])
        end_row = sb("end_row", [P, NV])
        n_pairs = sb("n_pairs", [P, NG])
        pair_end = sb("pair_end", [P, NG])
        shift = sb("shift", [P, NG])
        pair_no = sb("pair_no", [P, PK])
        group = sb("group", [P, PK])
        group_prev = sb("group_prev", [P, PK])
        pair_prev = sb("pair_prev", [P, PK])
        group8 = sb("group8", [P, PK])
        row_f = sb("row_f", [P, PK])
        row_c = sb("row_c", [P, PK])
        row_i = sb("row_i", [P, PK], I32)
        junk = sb("junk", [P, 2, NG])
        dst_e = sb("dst_e", [CW, PK, P], I32)
        src_e = sb("src_e", [CW, PK, P], I32)
        s_i = sb("s_i", [CW, PK, P], I32)
        d_f = sb("d_f", [CW, PK, P])
        m_f = sb("m_f", [CW, PK, P])
        t_f = sb("t_f", [CW, PK, P])
        t_i = sb("t_i", [CW, PK, P], I32)
        r_f = sb("r_f", [CW, PK, P])
        hits = sb("hits", [CW, 2, PK, P], BF16)
        pair_hits = sb("pair_hits", [CW, PK, GROUP])
        pair_hits_bf = sb("pair_hits_bf", [CW, PK, GROUP], BF16)
        group_iota = sb("group_iota", [P, NG])
        in_group = sb("in_group", [CW, 2, NG], BF16)
        deg_g = sb("deg_g", [CW, GB, GROUP])
        deg_t = sb("deg_t", [T, P])
        deg = sb("deg", [P, T])
        deg1 = sb("deg1", [P, T])
        half = sb("half", [P, T])
        code = sb("code", [P, PAIRS])
        low = sb("low", [P, PAIRS])
        tab = sb("tab", [P, 6, PK])
        tab_c = sb("tab_c", [P, 4, PK], I32)
        spare = sb("spare", [P, PK])
        s_slot = sb("s_slot", [P, PK], I32)
        tab_i = sb("tab_i", [1, 4, PAIRS], I32)
        code_iota = sb("code_iota", [P, CODES], F16)
        part = sb("part", [P, 1])
        one_hot = sb("one_hot", [P, BATCH, CODES + P], BF16)
        block_out = sb("block_out", [P, BATCH, CODES], BF16)

        s_tail = sem("tail_made")
        s_rows = sem("rows_written")
        s_ends = sem("ends_loaded")
        s_iota = sem("iotas_made")
        s_v = sem("prep_vector")
        s_below = sem("below_made")
        s_count = sem("rows_counted")
        s_row_i = sem("row_numbers")
        s_edges = sem("edges_gathered")
        s_hits = sem("pair_hits_made")
        s_in_group = sem("in_group_made")
        s_pe_group = sem("group_used")
        s_deg = sem("degrees_summed")
        s_deg_g = sem("degrees_copied")
        s_deg_out = sem("degrees_stored")
        s_deg_in = sem("degrees_loaded")
        s_deg_tr = sem("degrees_turned")
        s_codes = sem("codes_made")
        s_turn = sem("codes_turned")
        s_copied = sem("codes_copied")
        s_group_out = sem("groups_stored")
        s_group_in = sem("groups_loaded")
        s_tab = sem("tables_made")
        s_sqrt = sem("sqrt_done")
        s_half = sem("half_made")
        s_zero = sem("banks_zeroed")
        s_hot = sem("one_hot_ready")
        s_mm = sem("pair_multiplied")
        s_ev = sem("block_copied")
        s_st = [sem(f"block_stored{u}") for u in range(BATCH)]

        block = ctx.enter_context(nc.Block())
        TURN = 4

        def load(eng, ap, most):
            _, v = nc.values_load_multi_w_load_instructions(
                ap, engines=(eng.engine,), min_val=0, max_val=most,
                skip_runtime_bounds_check_because="the tables hold no others")
            return v

        def store_blocks(eng, b, slots):
            at = load(eng, tab_i[0:1, 3, bass.ds(b * BATCH, BATCH)], NG + BATCH - 1)
            for u in slots:
                eng.wait_ge(s_ev, b * BATCH + u + 1)
                eng.dma_start(counts[bass.ds(at[u], 1), :, :].rearrange("g p c -> p (g c)"),
                              block_out[:, u, :]).then_inc(s_st[u], 16)

        @block.sync
        def _(sp):
            flat_d = dst_rows.rearrange("r p -> (r p)")
            flat_s = src_rows.rearrange("r p -> (r p)")
            sp.dma_start(flat_d[0:E].rearrange("(a b) -> a b", a=16), a["dst"].rearrange("(a b) -> a b", a=16)).then_inc(s_rows, 16)
            sp.dma_start(flat_s[0:E].rearrange("(a b) -> a b", a=16), a["src"].rearrange("(a b) -> a b", a=16)).then_inc(s_rows, 16)
            sp.wait_ge(s_tail, 2)
            sp.dma_start(flat_d[E:].rearrange("(a b) -> a b", a=1), tail_dst[:]).then_inc(s_rows, 16)
            sp.dma_start(flat_s[E:].rearrange("(a b) -> a b", a=1), tail_src[:]).then_inc(s_rows, 16)
            sp.wait_ge(s_rows, 64)
            for j, e in enumerate((0, P - 1)):
                with nc.allow_non_contiguous_dma(reason="one number of each row"):
                    sp.dma_start(ends_i[:, j, :, :], dst_rows[:, e:e + 1].rearrange("(k q) o -> q k o", q=CW)).then_inc(s_ends, 16)
            sp.wait_ge(s_deg_g, 1)
            sp.dma_start(in_degree.rearrange("(b q d) -> q b d", q=CW, d=GROUP), deg_g[:]).then_inc(s_deg_out, 16)
            sp.wait_ge(s_deg_out, 16)
            sp.dma_start(deg_t[:], in_degree.rearrange("(t p) -> t p", p=P)).then_inc(s_deg_in, 16)
            sp.wait_ge(s_tab, 1)
            with nc.allow_non_contiguous_dma(reason="turns small tables"):
                for j in range(4):
                    sp.dma_start(pair_table[j].rearrange("(k q) -> q k", q=CW), tab_c[0:CW, j, :]).then_inc(s_group_out, 16)
            sp.wait_ge(s_group_out, 64)
            sp.dma_start(tab_i[:], pair_table.rearrange("(a j) b -> a j b", a=1)).then_inc(s_group_in, 16)
            sp.wait_ge(s_group_in, 16)

            with sp.Fori(0, PAIRS // BATCH) as b:
                store_blocks(sp, b, [u for u in range(BATCH) if u % 3 != 2])
            for u in range(BATCH):
                sp.wait_ge(s_st[u], 16 * (PAIRS // BATCH))

        @block.gpsimd
        def _(pool):
            nc.gpsimd.memset(tail_dst[:], PAD_DST).then_inc(s_tail, 1)
            nc.gpsimd.memset(tail_src[:], 0).then_inc(s_tail, 1)
            io = dict(allow_small_or_imprecise_dtypes=True)
            nc.gpsimd.iota(bounds[:], [[GROUP, NV]], base=0, channel_multiplier=0, **io).then_inc(s_iota, 1)
            nc.gpsimd.iota(pair_no[:], [[CW, PK]], base=0, channel_multiplier=1, **io).then_inc(s_iota, 1)
            nc.gpsimd.iota(part[:], [[0, 1]], base=0, channel_multiplier=1, **io).then_inc(s_iota, 1)
            nc.gpsimd.iota(code_iota[:], [[1, CODES]], base=0, channel_multiplier=0, **io).then_inc(s_iota, 1)
            nc.gpsimd.iota(group_iota[:], [[1, NG]], base=0, channel_multiplier=0, **io).then_inc(s_iota, 1)
            nc.gpsimd.iota(spare[:], [[0, PK]], base=0, channel_multiplier=1, **io).then_inc(s_iota, 1)
            pool.wait_ge(s_row_i, 1)
            for k in range(PK):
                for dst, table in ((dst_e, dst_rows), (src_e, src_rows)):
                    nc.gpsimd.indirect_dma_start(dst[:, k, :], None, table,
                                                 bass.IndirectOffsetOnAxis(row_i[0:CW, k:k + 1], 0)).then_inc(s_edges, 16)

            nc.gpsimd.memset(half[:], -0.5).then_inc(s_half, 1)
            pool.wait_ge(s_half, 1)
            pool.wait_ge(s_sqrt, 1)
            nc.gpsimd.tensor_tensor(deg_inv_sqrt[:], deg1[:], half[:], ALU.pow).then_inc(s_sqrt, 1)
            pool.wait_ge(s_group_in, 16)
            with pool.Fori(0, PAIRS // BATCH) as b:
                store_blocks(pool, b, [u for u in range(BATCH) if u % 3 == 2])

        @block.vector
        def _(dve):
            n = [0]

            def link(ins):
                n[0] += 1
                ins.then_inc(s_v, 1)
                dve.wait_ge(s_v, n[0])

            v = nc.vector
            v.memset(ones_bf[:], 1.0)
            v.memset(ones_row[:], 1.0)
            link(v.memset(zeros_bf[:], 0.0))
            dve.wait_ge(s_iota, 6)
            link(v.tensor_scalar(ident[:], group_iota[:, 0:P], part[:, 0:1], None, ALU.is_equal))
            dve.wait_ge(s_ends, 32)
            link(v.tensor_copy(ends[:].rearrange("q j k -> q (j k)"), ends_i[:].rearrange("q j k o -> q (j k o)")))
            for j in range(2 * CK):
                e = ends[:].rearrange("q j k -> q (j k)")[:, j:j + 1]
                last = v.tensor_scalar(below[:, j, :], bounds[0:CW, :], e, None, ALU.is_gt)
            last.then_inc(s_below, 1)
            dve.wait_ge(s_count, 1)
            v.tensor_copy(end_row[:], banks[:, 0:NV])
            link(v.tensor_copy(first_row[:], banks[:, 1024:1024 + NV]))
            link(v.tensor_tensor(n_pairs[:], end_row[:, 1:NV], first_row[:, 0:NG], ALU.subtract))
            link(v.tensor_scalar(n_pairs[:], n_pairs[:], 1.0, None, ALU.max))
            v.tensor_tensor_scan(pair_end[:], ones_row[:], n_pairs[:], 0.0, ALU.mult, ALU.add)
            link(v.tensor_tensor(shift[:], first_row[:, 1:NV], first_row[:, 0:NG], ALU.subtract))
            link(v.tensor_tensor(shift[:], shift[:], n_pairs[:], ALU.subtract))
            link(v.memset(shift[:, NG - 1:NG], 0.0))
            for k in range(PK):
                link(v.scalar_tensor_tensor(out=junk[0:CW, 0, :], in0=pair_end[0:CW, :], scalar=pair_no[0:CW, k:k + 1],
                                            in1=ones_row[0:CW, :], op0=ALU.is_le, op1=ALU.mult, accum_out=group[0:CW, k:k + 1]))
                link(v.scalar_tensor_tensor(out=junk[0:CW, 1, :], in0=pair_end[0:CW, :], scalar=pair_no[0:CW, k:k + 1],
                                            in1=shift[0:CW, :], op0=ALU.is_le, op1=ALU.mult, accum_out=row_f[0:CW, k:k + 1]))
            link(v.tensor_scalar(pair_prev[0:CW, :], pair_no[0:CW, :], 1.0, None, ALU.subtract))
            for k in range(PK):
                link(v.scalar_tensor_tensor(out=junk[0:CW, 0, :], in0=pair_end[0:CW, :], scalar=pair_prev[0:CW, k:k + 1],
                                            in1=ones_row[0:CW, :], op0=ALU.is_le, op1=ALU.mult, accum_out=group_prev[0:CW, k:k + 1]))
            tc, tf = tab_c[0:CW], tab[0:CW]
            v.tensor_copy(tc[:, 0, :], group[0:CW, :])
            v.tensor_scalar(tf[:, 0, :], group[0:CW, :], float(BANKS - 1), None, ALU.add)
            v.tensor_copy(s_slot[0:CW, :], spare[0:CW, :])
            link(v.tensor_tensor(tf[:, 1, :], group[0:CW, :], group_prev[0:CW, :], ALU.subtract))
            v.tensor_scalar(tf[:, 5, :], group[0:CW, :], 1.0, None, ALU.add)
            link(v.tensor_copy(tc[:, 1, :], tf[:, 0, :]))
            link(v.tensor_copy(tc[:, 2, :], tf[:, 5, :]))
            link(v.tensor_scalar(tc[:, 0:3, :], tc[:, 0:3, :], BANKS - 1, None, ALU.bitwise_and))
            link(v.tensor_scalar(tc[:, 0:3, :], tc[:, 0:3, :], BANK, None, ALU.mult))
            link(v.tensor_scalar(s_slot[0:CW, :], s_slot[0:CW, :], BATCH - 1, None, ALU.bitwise_and))
            link(v.tensor_scalar(tf[:, 2, :], s_slot[0:CW, :], float(NG), None, ALU.add))
            link(v.tensor_tensor(tf[:, 3, :], group[0:CW, :], tf[:, 2, :], ALU.subtract))
            link(v.scalar_tensor_tensor(out=tf[:, 4, :], in0=tf[:, 3, :], scalar=-1.0, in1=tf[:, 1, :], op0=ALU.add, op1=ALU.mult))
            v.tensor_tensor(tc[:, 3, :], tf[:, 4, :], tf[:, 2, :], ALU.add).then_inc(s_tab, 1)
            link(v.tensor_tensor(row_c[0:CW, :], row_f[0:CW, :], pair_no[0:CW, :], ALU.add))
            link(v.tensor_scalar(row_c[0:CW, :], row_c[0:CW, :], float(ROWS), None, ALU.min))
            v.tensor_copy(row_i[0:CW, :], row_c[0:CW, :]).then_inc(s_row_i, 1)
            v.tensor_scalar(group8[0:CW, :], group[0:CW, :], float(GROUP), None, ALU.mult).then_inc(s_row_i, 1)
            dve.wait_ge(s_row_i, 2)
            dve.wait_ge(s_edges, 32 * PK)
            v.tensor_scalar(s_i[:], src_e[:], 7, None, ALU.arith_shift_right)
            v.tensor_scalar(t_i[:], src_e[:], P - 1, None, ALU.bitwise_and)
            link(v.tensor_tensor(d_f[:], dst_e[:], group8[0:CW, :].unsqueeze(2).to_broadcast([CW, PK, P]), ALU.subtract))
            v.tensor_copy(r_f[:], t_i[:])
            link(v.tensor_scalar(m_f[:], d_f[:], 0.0, None, ALU.is_ge))
            link(v.scalar_tensor_tensor(out=t_f[:], in0=d_f[:], scalar=float(GROUP), in1=m_f[:], op0=ALU.is_lt, op1=ALU.mult))
            link(v.scalar_tensor_tensor(out=m_f[:], in0=s_i[:], scalar=float(GROUP), in1=d_f[:], op0=ALU.mult, op1=ALU.add))
            link(v.scalar_tensor_tensor(out=m_f[:], in0=m_f[:], scalar=1.0, in1=t_f[:], op0=ALU.add, op1=ALU.mult))
            link(v.tensor_scalar(m_f[:], m_f[:], 1.0, None, ALU.subtract))
            v.engine_nop().then_inc(s_codes, 1)
            for d in range(GROUP):
                h = hits[:, d % 2]
                link(v.tensor_scalar(h, d_f[:], float(d), None, ALU.is_equal))
                link(v.tensor_reduce(pair_hits[:, :, d:d + 1], h, mybir.AxisListType.X, ALU.add))
            v.tensor_copy(pair_hits_bf[:], pair_hits[:]).then_inc(s_hits, 1)
            for k in range(PK):
                if k >= 2:
                    dve.wait_ge(s_pe_group, k - 1)
                v.tensor_scalar(in_group[:, k % 2, :], group_iota[0:CW, :], group[0:CW, k:k + 1], None,
                                ALU.is_equal).then_inc(s_in_group, 1)
            dve.wait_ge(s_deg, 1)
            v.tensor_copy(deg_g[:].rearrange("q b d -> q (b d)"), banks[0:CW, 0:GB * GROUP]).then_inc(s_deg_g, 1)
            for j in range(2 * -(-PK // TURN)):
                k0 = (j // 2) * TURN
                w = min(TURN, PK - k0) * CW
                dve.wait_ge(s_turn, j + 1)
                v.tensor_copy((code, low)[j % 2][:, k0 * CW:k0 * CW + w], banks[:, (1 + j % 4) * BANK:(1 + j % 4) * BANK + w]).then_inc(s_copied, 1)
            dve.wait_ge(s_deg_tr, 1)
            v.tensor_scalar(deg[:], banks[:, 0:T], 1.0, None, ALU.max)
            v.tensor_scalar(deg1[:], banks[:, 0:T], 1.0, None, ALU.add).then_inc(s_sqrt, 1)
            dve.wait_ge(s_sqrt, 2)
            link(v.reciprocal(deg_inv[:], deg[:]))
            dve.wait_ge(s_group_in, 16)

            def turn(b_no, first):
                b = b_no * BATCH
                for u in range(BATCH):
                    if not first:
                        dve.wait_ge(s_mm, b + u - BATCH + 1)
                    v.tensor_scalar(one_hot[:, u, 0:CODES], code_iota[:], code[:, bass.ds(b + u, 1)], None, ALU.is_equal)
                    v.tensor_scalar(one_hot[:, u, CODES:], code_iota[:, 0:P], low[:, bass.ds(b + u, 1)], None,
                                    ALU.is_equal).then_inc(s_hot, 1)

            turn(0, True)
            with dve.Fori(1, PAIRS // BATCH) as b:
                turn(b, False)

        @block.scalar
        def _(act):
            act.wait_ge(s_group_in, 16)
            act.wait_ge(s_zero, 1)

            def turn(b_no, first):
                b = b_no * BATCH
                at = load(act, tab_i[0:1, 1, bass.ds(b, BATCH)], (BANKS - 1) * BANK)
                for u in range(BATCH):
                    if not first or u:
                        act.wait_ge(s_mm, b + u)
                    if not first:
                        act.wait_ge(s_st[u], b_no * 16)
                    nc.scalar.activation(block_out[:, u, :], banks[:, bass.ds(at[u], CODES)], ACT.Copy).then_inc(s_ev, 1)

            turn(0, True)
            with act.Fori(1, PAIRS // BATCH) as b:
                turn(b, False)

        @block.tensor
        def _(pe):
            pe.wait_ge(s_v, 1)
            pe.wait_ge(s_below, 1)
            for j in range(2):
                for lo, hi in ((0, BANK), (BANK, NV)):
                    for k in range(CK):
                        last = nc.tensor.matmul(banks[:, 1024 * j + lo:1024 * j + hi], ones_bf[0:CW, :],
                                                below[:, CK * j + k, lo:hi], start=(k == 0), stop=(k == CK - 1))
            last.then_inc(s_count, 1)
            pe.wait_ge(s_hits, 1)
            for k in range(PK):
                pe.wait_ge(s_in_group, k + 1)
                for b in range(GB):
                    last = nc.tensor.matmul(banks[0:CW, b * GROUP:(b + 1) * GROUP], in_group[:, k % 2, b * CW:(b + 1) * CW],
                                            pair_hits_bf[:, k, :], start=(k == 0 and b == 0), stop=(k == PK - 1), skip_group_check=True)
                last.then_inc(s_pe_group, 1)
            pe.wait_ge(s_pe_group, PK)
            nc.tensor.sem_inc(s_deg, 1)
            pe.wait_ge(s_codes, 1)
            for j in range(2 * -(-PK // TURN)):
                if j >= 4:
                    pe.wait_ge(s_copied, j - 3)
                k0 = (j // 2) * TURN
                for k in range(k0, min(k0 + TURN, PK)):
                    at = (1 + j % 4) * BANK + (k - k0) * CW
                    last = nc.tensor.transpose(banks[:, at:at + CW], (m_f, r_f)[j % 2][:, k, :], ident[0:CW, 0:CW])
                last.then_inc(s_turn, 1)
            pe.wait_ge(s_deg_in, 16)
            pe.wait_ge(s_deg_g, 1)
            nc.tensor.transpose(banks[:, 0:T], deg_t[:], ident[0:T, 0:T]).then_inc(s_deg_tr, 1)
            pe.wait_ge(s_sqrt, 1)
            pe.wait_ge(s_copied, 2 * -(-PK // TURN))
            for i in range(BANKS):
                last = nc.tensor.matmul(banks[:, i * BANK:(i + 1) * BANK], zeros_bf[:, 0:P], zeros_bf[:], start=True, stop=True)
            last.then_inc(s_zero, 1)
            pe.wait_ge(s_group_in, 16)

            def turn(b_no, first):
                b = b_no * BATCH
                at = load(pe, tab_i[0:1, 0, bass.ds(b, BATCH)], (BANKS - 1) * BANK)
                after = load(pe, tab_i[0:1, 2, bass.ds(b, BATCH)], (BANKS - 1) * BANK)
                for u in range(BATCH):
                    pe.wait_ge(s_hot, b + u + 1)
                    if not first or u >= 6:
                        pe.wait_ge(s_ev, b + u - 5)
                    nc.tensor.matmul(banks[:, bass.ds(after[u], 2)], zeros_bf[:, 0:P], zeros_bf[:, 0:2], start=True, stop=True, skip_group_check=True)
                    nc.tensor.matmul(banks[:, bass.ds(at[u], CODES)], one_hot[:, u, CODES:], one_hot[:, u, 0:CODES],
                                     start=False, stop=True, skip_group_check=True).then_inc(s_mm, 1)

            turn(0, True)
            with pe.Fori(1, PAIRS // BATCH) as b:
                turn(b, False)


def broadcast_row(ap):
    return bass.AP(tensor=ap.tensor, offset=ap.offset, ap=[[0, P]] + [list(x) for x in ap.ap])


def start_features(nc, a, g):
    T, N, D, H, KH, LAST, ident, banks, dis, feats, h_rows = (
        g[k] for k in ("T", "N", "D", "H", "KH", "LAST", "ident", "banks", "deg_inv_sqrt", "feats", "h_rows"))
    with ExitStack() as ctx:
        def sb(name, shape, dt=F32):
            return ctx.enter_context(nc.sbuf_tensor("i_" + name, shape, dt))

        def sem(name):
            return g["sem"](name)

        U = 7
        t_col = sb("t_col", [P, 1])
        w1_col = sb("w1_col", [P, KH])
        b1_col = sb("b1_col", [P, KH])
        time_w2 = sb("time_w2", [P, KH, H])
        b2_row = sb("b2_row", [P, H])
        inb_row = sb("inb_row", [P, H])
        in_w = sb("in_w", [P, H])
        hidden = sb("hidden", [P, KH])
        hidden_wide = sb("hidden_wide", [P, KH, P])
        c_row = sb("c_row", [P, H])
        x_in = sb("x_in", [P, U, D])
        x_t = sb("x_t", [P, U, D])
        h = sb("h", [P, U, H])
        y = sb("y", [P, U, H])
        parts = sb("parts", [P, U, 2 * H], F32R)
        s_w = sem("i_weights")
        s_hid = sem("i_hidden")
        s_wide = sem("i_wide")
        s_te = sem("i_time")
        s_c = sem("i_row")
        s_x = sem("i_x_loaded")
        s_zero = sem("i_zeroed")
        s_turn = sem("i_turned")
        s_xt = sem("i_turned_copied")
        s_mm = sem("i_multiplied")
        s_h = sem("i_h")
        s_y = sem("i_y")
        s_hi = sem("i_high")
        s_lo = sem("i_low")
        s_st = sem("i_stored")
        block = ctx.enter_context(nc.Block())
        TURNS = T // U
        x_v = a["x"][0:(T - 1) * P, :].rearrange("(t p) d -> p t d", p=P)
        f_v = feats.rearrange("(t p) f -> p t f", p=P)
        h_v = h_rows.rearrange("(t p) f -> p t f", p=P)

        @block.sync
        def _(sp):
            col = lambda v: v.rearrange("(k p) -> p k", p=P)
            with nc.allow_non_contiguous_dma(reason="small columns"):
                sp.dma_start(t_col[:], broadcast_row(a["L0_gnn_t"])).then_inc(s_w, 16)
                sp.dma_start(w1_col[:], col(a["L0_gnn_time_w1"].rearrange("o f -> (o f)"))).then_inc(s_w, 16)
                sp.dma_start(b1_col[:], col(a["L0_gnn_time_b1"])).then_inc(s_w, 16)
            sp.dma_start(time_w2[:], a["L0_gnn_time_w2"].rearrange("(k p) f -> p k f", p=P)).then_inc(s_w, 16)
            sp.dma_start(b2_row[:], broadcast_row(a["L0_gnn_time_b2"])).then_inc(s_w, 16)
            sp.dma_start(inb_row[:], broadcast_row(a["L0_gnn_in_b"])).then_inc(s_w, 16)
            sp.dma_start(in_w[:], a["L0_gnn_in_w"]).then_inc(s_w, 16)

            def store(b):
                sp.wait_ge(s_h, U * b + U)
                sp.dma_start(h_v[:, bass.ds(b * U, U), :], h[:]).then_inc(s_st, 16)
                sp.wait_ge(s_lo, U * b + U)
                sp.dma_start(f_v[:, bass.ds(b * U, U), :], parts[:].bitcast(F32)).then_inc(s_st, 16)

            sp.dma_start(x_in[:], x_v[:, 0:U, :]).then_inc(s_x, 16)
            store(0)
            with sp.Fori(1, TURNS - 1) as b:
                sp.wait_ge(s_st, 32 * b)
                sp.dma_start(x_in[:], x_v[:, bass.ds(b * U, U), :]).then_inc(s_x, 16)
                store(b)
            sp.wait_ge(s_st, 32 * (TURNS - 1))
            sp.dma_start(x_in[:, 0:U - 1, :], x_v[:, (TURNS - 1) * U:T - 1, :]).then_inc(s_x, 16)
            sp.wait_ge(s_zero, 1)
            sp.wait_ge(s_x, 16 * TURNS)
            sp.dma_start(x_in[0:LAST, U - 1, :], a["x"][(T - 1) * P:N, :]).then_inc(s_x, 16)
            store(TURNS - 1)
            sp.wait_ge(s_st, 32 * TURNS)

        @block.scalar
        def _(act):
            act.wait_ge(s_w, 16 * 7)
            for k in range(KH):
                ins = nc.scalar.activation(hidden[:, k:k + 1], w1_col[:, k:k + 1], ACT.Silu, bias=b1_col[:, k:k + 1], scale=t_col[:, 0:1])
            ins.then_inc(s_hid, 1)

            with act.Fori(0, TURNS) as b:
                for u in range(U):
                    act.wait_ge(s_turn, U * b + u + 1)
                    nc.scalar.activation(x_t[:, u, :], banks[:, u * BANK:u * BANK + P], ACT.Copy).then_inc(s_xt, 1)
                for u in range(U):
                    act.wait_ge(s_h, U * b + u + 1)
                    nc.scalar.activation(y[:, u, :], h[:, u, :], ACT.Copy, scale=dis[:, bass.ds(b * U + u, 1)]).then_inc(s_y, 1)
                for u in range(U):
                    act.wait_ge(s_y, U * b + u + 1)
                    nc.scalar.activation(parts[:, u, 0:H], y[:, u, :], ACT.Copy).then_inc(s_hi, 1)

        @block.tensor
        def _(pe):
            pe.wait_ge(s_wide, 1)
            for k in range(KH):
                ins = nc.tensor.matmul(banks[:, 7 * BANK:7 * BANK + H], hidden_wide[:, k, :], time_w2[:, k, :], start=(k == 0), stop=(k == KH - 1))
            ins.then_inc(s_te, 1)

            def turn(b, loads):
                pe.wait_ge(s_x, loads)
                for u in range(U):
                    nc.tensor.transpose(banks[:, u * BANK:u * BANK + P], x_in[:, u, :], ident[:]).then_inc(s_turn, 1)
                for u in range(U):
                    pe.wait_ge(s_xt, U * b + u + 1)
                    nc.tensor.matmul(banks[:, u * BANK + 128:u * BANK + 128 + H], x_t[:, u, :], in_w[:], start=True, stop=True).then_inc(s_mm, 1)

            turn(0, 16)
            with pe.Fori(1, TURNS - 1) as b:
                turn(b, 16 * b + 16)
            turn(TURNS - 1, 16 * TURNS + 16)

        @block.vector
        def _(dve):
            v = nc.vector
            dve.wait_ge(s_hid, 1)
            for k in range(KH):
                ins = v.tensor_copy(hidden_wide[:, k, :], hidden[:, k:k + 1].to_broadcast([P, P]))
            ins.then_inc(s_wide, 1)
            dve.wait_ge(s_w, 16 * 7)
            v.tensor_tensor(c_row[:], b2_row[:], inb_row[:], ALU.add).then_inc(s_c, 1)
            dve.wait_ge(s_c, 1)
            dve.wait_ge(s_te, 1)
            v.tensor_tensor(c_row[:], banks[:, 7 * BANK:7 * BANK + H], c_row[:], ALU.add).then_inc(s_c, 1)
            dve.wait_ge(s_c, 2)

            def turn(b, first):
                if not first:
                    dve.wait_ge(s_st, 32 * b)
                for u in range(U):
                    dve.wait_ge(s_mm, U * b + u + 1)
                    v.tensor_tensor(h[:, u, :], banks[:, u * BANK + 128:u * BANK + 128 + H], c_row[:], ALU.add).then_inc(s_h, 1)
                for u in range(U):
                    dve.wait_ge(s_hi, U * b + u + 1)
                    v.tensor_tensor(parts[:, u, H:], y[:, u, :], parts[:, u, 0:H].bitcast(F32), ALU.subtract).then_inc(s_lo, 1)

            turn(0, True)
            with dve.Fori(1, TURNS - 1) as b:
                turn(b, False)
            dve.wait_ge(s_turn, U * (TURNS - 1))
            v.memset(x_in[:, U - 1, :], 0.0).then_inc(s_zero, 1)
            turn(TURNS - 1, False)


class Counts:

    def __init__(self, nc, ctx, g, name):
        self.nc, self.g = nc, g
        T, self.PIECES, self.XB, self.TG, CODES = g["T"], g["PIECES"], g["XB"], g["TG"], g["CODES"]
        self.T = T
        self.packed = ctx.enter_context(nc.sbuf_tensor(name + "_packed", [P, 2, self.TG, CODES], BF16))
        self.wide = ctx.enter_context(nc.sbuf_tensor(name + "_wide", [P, self.PIECES, self.XB, P], F32R))
        self.loaded = [g["sem"](f"{name}_loaded{p}") for p in range(2)]
        self.made = [g["sem"](f"{name}_made{q}") for q in range(self.PIECES)]
        self.used = [g["sem"](f"{name}_used{q}") for q in range(self.PIECES)]

    def of_slot(self, r, m, p):
        return r * ((self.T + 1 - p) // 2) + m + 1

    def done(self, r, m, p):
        return r * self.T + 2 * m + p + 2

    def before(self, r, m, p):
        return r * self.T + 2 * m + p + 1

    def load(self, sp, r, m, p, first):
        for q in range(self.PIECES):
            sp.wait_ge(self.made[q], self.done(r, 0, -1) if first else self.done(r, m - 1, p))
        sp.dma_start(self.packed[:, p], self.g["counts"][bass.ds((2 * m + p) * self.TG, self.TG)].rearrange("g r c -> r g c")
                     ).then_inc(self.loaded[p], 16)

    def convert(self, eng, copy, r, m, p, q):
        if q in (0, 1):
            eng.wait_ge(self.loaded[p], 16 * self.of_slot(r, m, p))
        eng.wait_ge(self.used[q], self.before(r, m, p))
        w = self.XB * GROUP
        src = self.packed[:, p, :, q * w:(q + 1) * w].rearrange("r g (s d) -> r g s d", d=GROUP)
        dst = self.wide[:, q].rearrange("r s (g d) -> r g s d", d=GROUP)
        copy(dst, src).then_inc(self.made[q], 1)


def gcn_layers(nc, a, g):
    T, N, H, KH, L, PIECES, XB, ident, banks, dis, feats, h_rows = (
        g[k] for k in ("T", "N", "H", "KH", "L", "PIECES", "XB", "ident", "banks", "deg_inv_sqrt", "feats", "h_rows"))
    assert T % 2 == 1 and KH == 2
    with ExitStack() as ctx:
        def sb(name, shape, dt=F32):
            return ctx.enter_context(nc.sbuf_tensor("g_" + name, shape, dt))

        def sem(name):
            return g["sem"]("g_" + name)

        cnt = Counts(nc, ctx, g, "c")
        feat = sb("feat", [P, T, 2 * H], F32R)
        w_raw = sb("w_raw", [P, 3, KH, H])
        w = sb("w", [P, 3, KH, 2, H], F32R)
        rows = sb("rows", [P, 5, H])
        ln1 = sb("ln1", [P, 2, KH])
        ident_r = sb("ident_r", [P, P], F32R)
        consts = sb("consts", [P, 2])
        low_sum = sb("low_sum", [P, H])
        z = sb("z", [P, H])
        z_h, z_l = sb("z_h", [P, H], F32R), sb("z_l", [P, H], F32R)
        h_in = sb("h_in", [P, 2, H])
        h_b = sb("h_b", [P, H])
        h1 = sb("h1", [P, H])
        h1_h, h1_l = sb("h1_h", [P, H], F32R), sb("h1_l", [P, H], F32R)
        h1_be = sb("h1_be", [P, H])
        u1, n1, u2, n2 = (sb(x, [P, H]) for x in ("u1", "n1", "u2", "n2"))
        st1, st2 = sb("st1", [P, 6]), sb("st2", [P, 6])
        mv1, mv2 = sb("mv1", [P, 2]), sb("mv2", [P, 2])
        ve1, ve2 = sb("ve1", [P, 1]), sb("ve2", [P, 1])
        rs1, rs2 = sb("rs1", [P, 1]), sb("rs2", [P, 1])
        r_act = sb("r_act", [P, H])
        r_h, r_l = sb("r_h", [P, H], F32R), sb("r_l", [P, H], F32R)
        m2 = sb("m2", [P, H])
        h2 = sb("h2", [P, 2, H])
        y = sb("y", [P, H])
        parts = sb("parts", [P, 2, 2 * H], F32R)

        s_feat = [sem(f"feat_loaded{q}") for q in range(PIECES)]
        s_w = sem("weights_loaded")
        s_wh, s_wl = sem("weights_high"), sem("weights_low")
        s_const = sem("consts_made")
        s_hin = [sem(f"h_loaded{p}") for p in range(2)]
        s_st = [sem(f"tile_stored{p}") for p in range(2)]
        names = ("agg low z turn1 zh zl gcn hb h1 turn2 hh hl h1be res1 u1 st1 mv1 ve1 rs1 n1 turn3 r rh rl "
                 "res2 u2 st2 mv2 ve2 rs2 n2 m2 h2 y ph pl").split()
        S = {x: sem("s_" + x) for x in names}
        block = ctx.enter_context(nc.Block())
        bank = lambda i, w_: banks[:, i * BANK:i * BANK + w_]
        A0, B_T1, B_G, B_T2, B_R1, B_T3, B_R2 = 0, 2, 3, 4, 5, 6, 7
        GCN_B, B1, B2, G2, BE2 = range(5)
        done, before = cnt.done, cnt.before
        DVE_PIECES = (1, 3, 5)
        W_NAMES = ("L0_gnn_gcn_w", "L0_gnn_res_w1", "L0_gnn_res_w2")
        R_NAMES = ("L0_gnn_gcn_b", "L0_gnn_res_b1", "L0_gnn_res_b2", "L0_gnn_res_g2", "L0_gnn_res_be2")
        LOADS = len(W_NAMES) + len(R_NAMES) + 2

        def credit(eng, sems):
            for s in sems:
                eng.sem_inc(s, 1)

        def layer(eng, l, body, before_tiles=None):
            if before_tiles:
                before_tiles(l)
            M = T // 2
            body(l, (0, 0), None, None)
            body(l, (0, 1), (0, 0), None)
            with eng.Fori(1, M) as m:
                body(l, (m, 0), (m - 1, 1), (m - 1, 0))
                body(l, (m, 1), (m, 0), (m - 1, 1))
            body(l, (M, 0), (M - 1, 1), (M - 1, 0))
            body(l, None, (M, 0), (M - 1, 1))
            body(l, None, None, (M, 0))

        def nxt(tile):
            m, p = tile
            if isinstance(m, int) and 2 * m + p == T - 1:
                return None
            return (m, 1) if p == 0 else (m + 1, 0)

        def early(tile):
            return isinstance(tile[0], int) and tile[0] == 0

        @block.sync
        def _(sp):
            def start(l):
                def weight(j):
                    sp.dma_start(w_raw[:, j], a[W_NAMES[j]][bass.ds(l, 1)].rearrange("o (k p) f -> p (o k) f", p=P)).then_inc(s_w, 16)

                sp.wait_ge(s_st[0], 32 * l * ((T + 1) // 2) + 1)
                weight(0)
                sp.wait_ge(s_st[1], 32 * l * (T // 2) + 1)
                for q in range(PIECES):
                    s0 = q * XB
                    sp.dma_start(feat[:, s0:s0 + XB, :].bitcast(F32), feats[s0 * P:(s0 + XB) * P, :].rearrange("(s p) f -> p s f", p=P)
                                 ).then_inc(s_feat[q], 16)
                    if q == 0:
                        cnt.load(sp, l, 0, 0, True)
                weight(1)
                weight(2)
                for j, n in enumerate(R_NAMES):
                    sp.dma_start(rows[:, j], a[n][bass.ds(l, 1), :].to_broadcast([P, H])).then_inc(s_w, 16)
                with nc.allow_non_contiguous_dma(reason="small columns"):
                    for j, n in enumerate(("L0_gnn_res_g1", "L0_gnn_res_be1")):
                        sp.dma_start(ln1[:, j], a[n][bass.ds(l, 1), :].rearrange("o (k p) -> p (o k)", p=P)).then_inc(s_w, 16)

            def body(l, t, d1, d2):
                if t is not None:
                    m, p = t
                    if early(t):
                        sp.wait_ge(S["hb"], before(l, 0, 0))
                    else:
                        sp.wait_ge(S["hb"], done(l, m - 1, p))
                    sp.dma_start(h_in[:, p], h_rows[bass.ds((2 * m + p) * P, P), :]).then_inc(s_hin[p], 16)
                    n = nxt(t)
                    if n is not None:
                        cnt.load(sp, l, n[0], n[1], isinstance(n[0], int) and n[0] == 0)
                if d2 is not None:
                    m, p = d2
                    sp.wait_ge(S["h2"], done(l, m, p))
                    sp.dma_start(h_rows[bass.ds((2 * m + p) * P, P), :], h2[:, p]).then_inc(s_st[p], 16)
                    sp.wait_ge(S["pl"], done(l, m, p))
                    sp.dma_start(feats[bass.ds((2 * m + p) * P, P), :], parts[:, p].bitcast(F32)).then_inc(s_st[p], 16)

            credit(sp, s_st)
            with sp.Fori(0, L) as l:
                layer(sp, l, body, start)
            for p in range(2):
                sp.wait_ge(s_st[p], 32 * L * ((T + 1 - p) // 2) + 1)

        @block.tensor
        def _(pe):
            credit(pe, cnt.used + [S[x] for x in "agg turn1 gcn turn2 res1 turn3 res2".split()])
            pe.wait_ge(s_const, 1)

            def turn(to, src, s, l, t, needs):
                for x in needs:
                    pe.wait_ge(S[x], done(l, *t))
                for k in range(KH):
                    ins = nc.tensor.transpose(banks[:, to * BANK + k * P:to * BANK + (k + 1) * P], src[:, k * P:(k + 1) * P], ident[:])
                ins.then_inc(S[s], 1)

            def product(to, hi, lo, j, s, l, t, needs):
                for x in needs:
                    pe.wait_ge(S[x], done(l, *t))
                n = 0
                for k in range(KH):
                    for left, part in ((hi, 0), (hi, 1), (lo, 0)):
                        n += 1
                        ins = nc.tensor.matmul(bank(to, H), left[:, k * P:(k + 1) * P], w[:, j, k, part, :],
                                               start=(n == 1), stop=(n == 3 * KH))
                ins.then_inc(S[s], 1)

            def body(l, t, d1, d2):
                def piece(q):
                    if t is None:
                        return
                    m, p = t
                    if q == 0 and not early(t):
                        pe.wait_ge(S["z"], done(l, m - 1, p))
                    pe.wait_ge(cnt.made[q], done(l, m, p))
                    if early(t) and p == 0:
                        pe.wait_ge(s_feat[q], 16 * (l + 1))
                    for s in range(XB):
                        ins = nc.tensor.matmul(bank(p, 2 * H), cnt.wide[:, q, s, :], feat[:, q * XB + s, :],
                                               start=(q == 0 and s == 0), stop=False)
                    ins.then_inc(cnt.used[q], 1)
                    if q == PIECES - 1:
                        nc.tensor.matmul(bank(p, 2 * H), ident_r[:], feat[:, bass.ds(2 * m + p, 1), :].rearrange("p o f -> p (o f)"),
                                         start=False, stop=True).then_inc(S["agg"], 1)

                piece(0)
                if d1 is not None:
                    turn(B_T1, z, "turn1", l, d1, ["z"])
                piece(1)
                if d2 is not None:
                    product(B_R2, r_h, r_l, 2, "res2", l, d2, ["rh", "rl"])
                piece(2)
                if d1 is not None:
                    if early(d1) and d1[1] == 0:
                        pe.wait_ge(s_wh, l + 1)
                        pe.wait_ge(s_wl, l + 1)
                    product(B_G, z_h, z_l, 0, "gcn", l, d1, ["zh", "zl"])
                piece(3)
                if d1 is not None:
                    turn(B_T2, h1, "turn2", l, d1, ["h1"])
                piece(4)
                if d1 is not None:
                    product(B_R1, h1_h, h1_l, 1, "res1", l, d1, ["hh", "hl"])
                piece(5)
                piece(6)
                if d1 is not None:
                    turn(B_T3, n1, "turn3", l, d1, ["n1"])

            with pe.Fori(0, L) as l:
                layer(pe, l, body)

        @block.scalar
        def _(act):
            credit(act, [cnt.made[q] for q in range(PIECES) if q not in DVE_PIECES])
            credit(act, [S[x] for x in "low zh hh r rh y ph".split()])
            s = nc.scalar

            def conv(l, t, q):
                if t is not None:
                    cnt.convert(act, lambda d, x: s.activation(d, x, ACT.Copy), l, t[0], t[1], q)

            def wait(x, l, t):
                act.wait_ge(S[x], done(l, *t))

            def start(l):
                for q in range(PIECES):
                    if q not in DVE_PIECES:
                        conv(l, (0, 0), q)
                act.wait_ge(s_w, 16 * LOADS * (l + 1))
                act.wait_ge(S["res2"], l * T + 1)
                for j in range(3):
                    ins = s.activation(w[:, j, :, 0, :], w_raw[:, j], ACT.Copy)
                ins.then_inc(s_wh, 1)

            def body(l, t, d1, d2):
                n = nxt(t) if t is not None else None
                if d1 is not None:
                    act.wait_ge(s_const, 1)
                    wait("agg", l, d1)
                    s.activation(low_sum[:], banks[:, d1[1] * BANK + H:(d1[1] + 1) * BANK], ACT.Copy,
                                 scale=dis[:, bass.ds(2 * d1[0] + d1[1], 1)]).then_inc(S["low"], 1)
                if d2 is not None:
                    wait("turn3", l, d2)
                    for k in range(KH):
                        ins = s.activation(r_act[:, k * P:(k + 1) * P], banks[:, B_T3 * BANK + k * P:B_T3 * BANK + (k + 1) * P],
                                           ACT.Silu, bias=ln1[:, 1, k:k + 1], scale=ln1[:, 0, k:k + 1])
                    ins.then_inc(S["r"], 1)
                    wait("r", l, d2)
                    s.activation(r_h[:], r_act[:], ACT.Copy).then_inc(S["rh"], 1)
                if d1 is not None:
                    wait("turn1", l, d1)
                    s.activation(z_h[:], bank(B_T1, H), ACT.Copy).then_inc(S["zh"], 1)
                conv(l, n, 0)
                conv(l, n, 2)
                if d1 is not None:
                    wait("turn2", l, d1)
                    s.activation(h1_h[:], bank(B_T2, H), ACT.Copy).then_inc(S["hh"], 1)
                conv(l, n, 4)
                if d2 is not None:
                    m, p = d2
                    act.wait_ge(s_const, 1)
                    wait("h2", l, d2)
                    s.activation(y[:], h2[:, p], ACT.Copy, scale=dis[:, bass.ds(2 * m + p, 1)]).then_inc(S["y"], 1)
                    wait("y", l, d2)
                    if not early(d2):
                        act.wait_ge(s_st[p], 32 * (cnt.of_slot(l, m, p) - 1) + 1)
                    s.activation(parts[:, p, 0:H], y[:], ACT.Copy).then_inc(S["ph"], 1)
                conv(l, n, 6)

            with act.Fori(0, L) as l:
                layer(act, l, body, start)

        @block.vector
        def _(dve):
            v = nc.vector
            credit(dve, [cnt.made[q] for q in DVE_PIECES])
            credit(dve, [S[x] for x in "z zl h1 hl u1 st1 mv1 n1 rl u2 st2 mv2 n2 h2 pl".split()])
            v.memset(consts[:, 0:1], -0.5)
            v.tensor_copy(ident_r[:], ident[:]).then_inc(s_const, 1)

            def conv(l, t, q):
                if t is not None:
                    cnt.convert(dve, v.tensor_copy, l, t[0], t[1], q)

            def wait(l, t, *xs):
                for x in xs:
                    dve.wait_ge(S[x], done(l, *t))

            def start(l):
                for q in DVE_PIECES:
                    conv(l, (0, 0), q)
                dve.wait_ge(s_wh, l + 1)
                for j in range(3):
                    ins = v.tensor_tensor(w[:, j, :, 1, :], w_raw[:, j], w[:, j, :, 0, :].bitcast(F32), ALU.subtract)
                ins.then_inc(s_wl, 1)

            def body(l, t, d1, d2):
                n = nxt(t) if t is not None else None
                if d1 is not None:
                    wait(l, d1, "low")
                    v.scalar_tensor_tensor(out=z[:], in0=bank(d1[1], H), scalar=dis[:, bass.ds(2 * d1[0] + d1[1], 1)],
                                           in1=low_sum[:], op0=ALU.mult, op1=ALU.add).then_inc(S["z"], 1)
                if d2 is not None:
                    wait(l, d2, "rh")
                    v.tensor_tensor(r_l[:], r_act[:], r_h[:].bitcast(F32), ALU.subtract).then_inc(S["rl"], 1)
                if d1 is not None:
                    wait(l, d1, "zh")
                    v.tensor_tensor(z_l[:], bank(B_T1, H), z_h[:].bitcast(F32), ALU.subtract).then_inc(S["zl"], 1)
                conv(l, n, 1)
                if d2 is not None:
                    wait(l, d2, "res2")
                    v.tensor_tensor(u2[:], bank(B_R2, H), rows[:, B2], ALU.add).then_inc(S["u2"], 1)
                    wait(l, d2, "u2")
                    v.bn_stats(st2[:], u2[:]).then_inc(S["st2"], 1)
                    dve.wait_ge(s_const, 1)
                    wait(l, d2, "st2")
                    v.bn_aggr(mv2[:], st2[:]).then_inc(S["mv2"], 1)
                if d1 is not None:
                    wait(l, d1, "gcn", "hb")
                    v.tensor_tensor(h1[:], bank(B_G, H), h_b[:], ALU.add).then_inc(S["h1"], 1)
                if d2 is not None:
                    wait(l, d2, "rs2", "mv2")
                    v.tensor_scalar(n2[:], u2[:], mv2[:, 0:1], rs2[:, 0:1], ALU.subtract, ALU.mult).then_inc(S["n2"], 1)
                if d1 is not None:
                    wait(l, d1, "hh")
                    v.tensor_tensor(h1_l[:], bank(B_T2, H), h1_h[:].bitcast(F32), ALU.subtract).then_inc(S["hl"], 1)
                conv(l, n, 3)
                if d2 is not None:
                    m, p = d2
                    wait(l, d2, "m2", "h1be")
                    if not early(d2):
                        dve.wait_ge(s_st[p], 32 * (cnt.of_slot(l, m, p) - 1) + 1)
                    v.tensor_tensor(h2[:, p], m2[:], h1_be[:], ALU.add).then_inc(S["h2"], 1)
                if d1 is not None:
                    wait(l, d1, "res1")
                    v.tensor_tensor(u1[:], bank(B_R1, H), rows[:, B1], ALU.add).then_inc(S["u1"], 1)
                    wait(l, d1, "u1")
                    v.bn_stats(st1[:], u1[:]).then_inc(S["st1"], 1)
                    dve.wait_ge(s_const, 1)
                    wait(l, d1, "st1")
                    v.bn_aggr(mv1[:], st1[:]).then_inc(S["mv1"], 1)
                if d2 is not None:
                    m, p = d2
                    wait(l, d2, "ph")
                    v.tensor_tensor(parts[:, p, H:], y[:], parts[:, p, 0:H].bitcast(F32), ALU.subtract).then_inc(S["pl"], 1)
                if d1 is not None:
                    wait(l, d1, "rs1", "mv1")
                    v.tensor_scalar(n1[:], u1[:], mv1[:, 0:1], rs1[:, 0:1], ALU.subtract, ALU.mult).then_inc(S["n1"], 1)
                conv(l, n, 5)

            with dve.Fori(0, L) as l:
                layer(dve, l, body, start)

        @block.gpsimd
        def _(pool):
            gp = nc.gpsimd
            credit(pool, [S[x] for x in "hb h1be ve1 rs1 ve2 rs2 m2".split()])
            pool.wait_ge(s_const, 1)

            def wait(l, t, *xs):
                for x in xs:
                    pool.wait_ge(S[x], done(l, *t))

            def start(l):
                pool.wait_ge(s_w, 16 * LOADS * (l + 1))

            def root(l, t, j, mv, ve, rs):
                pool.wait_ge(s_const, 1)
                wait(l, t, f"mv{j}")
                gp.tensor_scalar(ve[:], mv[:, 1:2], EPS, None, ALU.add).then_inc(S[f"ve{j}"], 1)
                wait(l, t, f"ve{j}")
                gp.tensor_tensor(rs[:], ve[:], consts[:, 0:1], ALU.pow).then_inc(S[f"rs{j}"], 1)

            def body(l, t, d1, d2):
                if d1 is not None:
                    m, p = d1
                    pool.wait_ge(s_hin[p], 16 * cnt.of_slot(l, m, p))
                    pool.wait_ge(S["h1"], before(l, m, p))
                    gp.tensor_tensor(h_b[:], h_in[:, p], rows[:, GCN_B], ALU.add).then_inc(S["hb"], 1)
                if d2 is not None:
                    root(l, d2, 2, mv2, ve2, rs2)
                    wait(l, d2, "n2")
                    gp.tensor_tensor(m2[:], n2[:], rows[:, G2], ALU.mult).then_inc(S["m2"], 1)
                if d1 is not None:
                    wait(l, d1, "h1")
                    pool.wait_ge(S["h2"], before(l, *d1))
                    gp.tensor_tensor(h1_be[:], h1[:], rows[:, BE2], ALU.add).then_inc(S["h1be"], 1)
                    root(l, d1, 1, mv1, ve1, rs1)

            with pool.Fori(0, L) as l:
                layer(pool, l, body, start)


def output_mlp(nc, a, g):
    T, N, D, H, KH, LAST, ident, banks, h_rows, x1_rows = (
        g[k] for k in ("T", "N", "D", "H", "KH", "LAST", "ident", "banks", "h_rows", "x1_rows"))
    with ExitStack() as ctx:
        def sb(name, shape, dt=F32):
            return ctx.enter_context(nc.sbuf_tensor("o_" + name, shape, dt))

        def sem(name):
            return g["sem"]("o_" + name)

        U = 7
        TURNS = T // U
        w1_raw, w2_raw = sb("w1_raw", [P, KH, H]), sb("w2_raw", [P, KH, D])
        w1, w2 = sb("w1", [P, KH, 2, H], F32R), sb("w2", [P, KH, 2, D], F32R)
        b1, b2 = sb("b1", [P, H]), sb("b2", [P, D])
        half = sb("half", [P, U])
        h_in, x_in = sb("h_in", [P, 2, U, H]), sb("x_in", [P, 2, U, D])
        a_h, a_l = sb("a_h", [P, U, H], F32R), sb("a_l", [P, U, H], F32R)
        mid, act_mid = sb("mid", [P, U, H]), sb("act_mid", [P, U, H])
        c_h, c_l = sb("c_h", [P, U, H], F32R), sb("c_l", [P, U, H], F32R)
        xb, f = sb("xb", [P, U, D]), sb("f", [P, U, D])
        st, mv, ve, rs = sb("st", [P, U, 6]), sb("mv", [P, U, 2]), sb("ve", [P, U]), sb("rs", [P, U])
        x1 = sb("x1", [P, U, D])
        parts = sb("parts", [P, U, 2 * D], F32R)
        s_in = [sem(f"in{p}") for p in range(2)]
        S = {x: sem(x) for x in "w b wh wl const zero turn1 ah al mm1 mid silu turn2 ch cl mm2 xb f st mv ve rs x1 ph pl out".split()}
        block = ctx.enter_context(nc.Block())
        h_v = h_rows.rearrange("(t p) f -> p t f", p=P)
        x_v = a["x"][0:(T - 1) * P, :].rearrange("(t p) d -> p t d", p=P)
        o_v = x1_rows.rearrange("(t p) f -> p t f", p=P)

        @block.sync
        def _(sp):
            sp.dma_start(w1_raw[:], a["L0_gnn_out_w1"].rearrange("(k p) f -> p k f", p=P)).then_inc(S["w"], 16)
            sp.dma_start(w2_raw[:], a["L0_gnn_out_w2"].rearrange("(k p) f -> p k f", p=P)).then_inc(S["w"], 16)
            sp.dma_start(b1[:], broadcast_row(a["L0_gnn_out_b1"])).then_inc(S["b"], 16)
            sp.dma_start(b2[:], broadcast_row(a["L0_gnn_out_b2"])).then_inc(S["b"], 16)
            sp.wait_ge(S["zero"], 1)
            for b in range(TURNS):
                if b >= 2:
                    sp.wait_ge(S["xb"], b - 1)
                    sp.wait_ge(S["turn1"], U * (b - 1))
                if b < TURNS - 1:
                    sp.dma_start(x_in[:, b % 2], x_v[:, b * U:(b + 1) * U, :]).then_inc(s_in[b % 2], 16)
                else:
                    sp.dma_start(x_in[:, b % 2, 0:U - 1], x_v[:, b * U:T - 1, :]).then_inc(s_in[b % 2], 16)
                    sp.dma_start(x_in[0:LAST, b % 2, U - 1], a["x"][(T - 1) * P:N, :]).then_inc(s_in[b % 2], 16)
                sp.dma_start(h_in[:, b % 2], h_v[:, b * U:(b + 1) * U, :]).then_inc(s_in[b % 2], 16)
                if b:
                    sp.wait_ge(S["pl"], b)
                    sp.dma_start(o_v[:, (b - 1) * U:b * U, :], parts[:].bitcast(F32)).then_inc(S["out"], 16)
            sp.wait_ge(S["pl"], TURNS)
            sp.dma_start(o_v[:, (TURNS - 1) * U:, :], parts[:].bitcast(F32)).then_inc(S["out"], 16)
            sp.wait_ge(S["out"], 16 * TURNS)

        loaded = lambda b: 32 * (b // 2 + 1) + 16 * (b == TURNS - 1)
        left, right = lambda u, w: banks[:, u * BANK:u * BANK + w], lambda u, w: banks[:, u * BANK + 256:u * BANK + 256 + w]

        @block.tensor
        def _(pe):
            def turn(b, src, s):
                for u in range(U):
                    for k in range(KH):
                        ins = nc.tensor.transpose(banks[:, u * BANK + k * P:u * BANK + (k + 1) * P], src[:, u, k * P:(k + 1) * P], ident[:])
                    ins.then_inc(S[s], 1)

            def product(b, hi, lo, w, width, need_h, need_l, s):
                for u in range(U):
                    pe.wait_ge(S[need_h], U * b + u + 1)
                    pe.wait_ge(S[need_l], U * b + u + 1)
                    n = 0
                    for k in range(KH):
                        for x, part in ((hi, 0), (hi, 1), (lo, 0)):
                            n += 1
                            ins = nc.tensor.matmul(right(u, width), x[:, u, k * P:(k + 1) * P], w[:, k, part, :], start=(n == 1), stop=(n == 6))
                    ins.then_inc(S[s], 1)

            pe.wait_ge(S["wl"], 1)
            for b in range(TURNS):
                pe.wait_ge(s_in[b % 2], loaded(b))
                if b:
                    pe.wait_ge(S["f"], U * b)
                turn(b, h_in[:, b % 2], "turn1")
                product(b, a_h, a_l, w1, H, "ah", "al", "mm1")
                for u in range(U):
                    pe.wait_ge(S["silu"], U * b + u + 1)
                    for k in range(KH):
                        ins = nc.tensor.transpose(banks[:, u * BANK + k * P:u * BANK + (k + 1) * P], act_mid[:, u, k * P:(k + 1) * P], ident[:])
                    ins.then_inc(S["turn2"], 1)
                product(b, c_h, c_l, w2, D, "ch", "cl", "mm2")

        @block.scalar
        def _(act):
            s = nc.scalar
            act.wait_ge(S["w"], 32)
            s.activation(w1[:, :, 0, :], w1_raw[:], ACT.Copy)
            s.activation(w2[:, :, 0, :], w2_raw[:], ACT.Copy).then_inc(S["wh"], 1)
            for b in range(TURNS):
                for u in range(U):
                    act.wait_ge(S["turn1"], U * b + u + 1)
                    s.activation(a_h[:, u], left(u, H), ACT.Copy).then_inc(S["ah"], 1)
                for u in range(U):
                    act.wait_ge(S["mid"], U * b + u + 1)
                    s.activation(act_mid[:, u], mid[:, u], ACT.Silu).then_inc(S["silu"], 1)
                for u in range(U):
                    act.wait_ge(S["turn2"], U * b + u + 1)
                    s.activation(c_h[:, u], left(u, H), ACT.Copy).then_inc(S["ch"], 1)
                act.wait_ge(S["x1"], b + 1)
                if b:
                    act.wait_ge(S["out"], 16 * b)
                s.activation(parts[:, :, 0:D], x1[:], ACT.Copy).then_inc(S["ph"], 1)

        @block.vector
        def _(dve):
            v = nc.vector
            v.memset(half[:], -0.5).then_inc(S["const"], 1)
            v.memset(x_in[:, (TURNS - 1) % 2, U - 1, :], 0.0).then_inc(S["zero"], 1)
            dve.wait_ge(S["wh"], 1)
            v.tensor_tensor(w1[:, :, 1, :], w1_raw[:], w1[:, :, 0, :].bitcast(F32), ALU.subtract)
            v.tensor_tensor(w2[:, :, 1, :], w2_raw[:], w2[:, :, 0, :].bitcast(F32), ALU.subtract).then_inc(S["wl"], 1)
            dve.wait_ge(S["b"], 32)
            for b in range(TURNS):
                for u in range(U):
                    dve.wait_ge(S["ah"], U * b + u + 1)
                    v.tensor_tensor(a_l[:, u], left(u, H), a_h[:, u].bitcast(F32), ALU.subtract).then_inc(S["al"], 1)
                for u in range(U):
                    dve.wait_ge(S["mm1"], U * b + u + 1)
                    v.tensor_tensor(mid[:, u], right(u, H), b1[:], ALU.add).then_inc(S["mid"], 1)
                for u in range(U):
                    dve.wait_ge(S["ch"], U * b + u + 1)
                    v.tensor_tensor(c_l[:, u], left(u, H), c_h[:, u].bitcast(F32), ALU.subtract).then_inc(S["cl"], 1)
                dve.wait_ge(S["xb"], b + 1)
                for u in range(U):
                    dve.wait_ge(S["mm2"], U * b + u + 1)
                    v.tensor_tensor(f[:, u], right(u, D), xb[:, u], ALU.add).then_inc(S["f"], 1)
                for u in range(U):
                    dve.wait_ge(S["f"], U * b + u + 1)
                    v.bn_stats(st[:, u], f[:, u]).then_inc(S["st"], 1)
                for u in range(U):
                    dve.wait_ge(S["st"], U * b + u + 1)
                    v.bn_aggr(mv[:, u], st[:, u]).then_inc(S["mv"], 1)
                dve.wait_ge(S["rs"], b + 1)
                for u in range(U):
                    dve.wait_ge(S["mv"], U * b + u + 1)
                    ins = v.tensor_scalar(x1[:, u], f[:, u], mv[:, u, 0:1], rs[:, u:u + 1], ALU.subtract, ALU.mult)
                ins.then_inc(S["x1"], 1)
                dve.wait_ge(S["x1"], b + 1)
                dve.wait_ge(S["ph"], b + 1)
                v.tensor_tensor(parts[:, :, D:], x1[:], parts[:, :, 0:D].bitcast(F32), ALU.subtract).then_inc(S["pl"], 1)

        @block.gpsimd
        def _(pool):
            gp = nc.gpsimd
            pool.wait_ge(S["b"], 32)
            pool.wait_ge(S["const"], 1)
            for b in range(TURNS):
                pool.wait_ge(s_in[b % 2], loaded(b))
                if b:
                    pool.wait_ge(S["f"], U * b)
                gp.tensor_tensor(xb[:], x_in[:, b % 2], b2[:].unsqueeze(1).to_broadcast([P, U, D]), ALU.add).then_inc(S["xb"], 1)
                pool.wait_ge(S["mv"], U * (b + 1))
                gp.tensor_scalar(ve[:], mv[:, :, 1], EPS, None, ALU.add).then_inc(S["ve"], 1)
                pool.wait_ge(S["ve"], b + 1)
                gp.tensor_tensor(rs[:], ve[:], half[:], ALU.pow).then_inc(S["rs"], 1)


def sage_layer(nc, a, g):
    T, N, D, LAST, PIECES, XB, ident, banks, deg_inv, x1_rows, out = (
        g[k] for k in ("T", "N", "D", "LAST", "PIECES", "XB", "ident", "banks", "deg_inv", "x1_rows", "out"))
    with ExitStack() as outer:
        feat = outer.enter_context(nc.sbuf_tensor("s_feat", [P, T, 2 * D], F32R))
        act_h = outer.enter_context(nc.sbuf_tensor("s_act_h", [P, T, D], F32))
        with ExitStack() as ctx:
            def sb(name, shape, dt=F32):
                return ctx.enter_context(nc.sbuf_tensor("s_" + name, shape, dt))

            def sem(name):
                return g["sem"]("s1_" + name)

            cnt = Counts(nc, ctx, g, "d")
            w_raw = sb("w_raw", [P, 2, D])
            w_t = sb("w_t", [P, 2, D])
            w = sb("w", [P, 2, 2, D], F32R)
            b_row = sb("b_row", [P, D])
            low_sum = sb("low_sum", [P, D])
            both = sb("both", [P, 2, D])
            b_h, b_l = sb("b_h", [P, 2 * D], F32R), sb("b_l", [P, 2 * D], F32R)
            pre = sb("pre", [P, D])
            s_feat = [sem(f"feat_loaded{q}") for q in range(PIECES)]
            s_w, s_wt, s_wtc, s_wh, s_wl = (sem(x) for x in ("w", "wt", "wtc", "wh", "wl"))
            S = {x: sem(x) for x in "low mean own turn bh bl prod pre relu".split()}
            block = ctx.enter_context(nc.Block())
            done, before = cnt.done, cnt.before
            DVE_PIECES = (1, 3, 5)
            M = T // 2

            def turns(eng, body):
                body((0, 0), None)
                body((0, 1), (0, 0))
                with eng.Fori(1, M) as m:
                    body((m, 0), (m - 1, 1))
                    body((m, 1), (m, 0))
                body((M, 0), (M - 1, 1))
                body(None, (M, 0))

            def nxt(tile):
                m, p = tile
                if isinstance(m, int) and 2 * m + p == T - 1:
                    return None
                return (m, 1) if p == 0 else (m + 1, 0)

            def early(t):
                return isinstance(t[0], int) and t[0] == 0

            def credit(eng, sems):
                for s in sems:
                    eng.sem_inc(s, 1)

            @block.sync
            def _(sp):
                for j, n in enumerate(("L1_gnn_W_l", "L1_gnn_W_r")):
                    sp.dma_start(w_raw[:, j], a[n]).then_inc(s_w, 16)
                sp.dma_start(b_row[:], broadcast_row(a["L1_gnn_b"])).then_inc(s_w, 16)
                cnt.load(sp, 0, 0, 0, True)
                for q in range(PIECES):
                    s0 = q * XB
                    sp.dma_start(feat[:, s0:s0 + XB, :].bitcast(F32), x1_rows[s0 * P:(s0 + XB) * P, :].rearrange("(s p) f -> p s f", p=P)
                                 ).then_inc(s_feat[q], 16)

                def body(t, d1):
                    n = nxt(t) if t is not None else None
                    if n is not None:
                        cnt.load(sp, 0, n[0], n[1], isinstance(n[0], int) and n[0] == 0)

                turns(sp, body)

            @block.tensor
            def _(pe):
                credit(pe, cnt.used + [S[x] for x in "turn prod".split()])
                pe.wait_ge(s_w, 48)
                for j in range(2):
                    ins = nc.tensor.transpose(banks[:, 7 * BANK + j * P:7 * BANK + (j + 1) * P], w_raw[:, j], ident[:])
                ins.then_inc(s_wt, 1)

                def body(t, d1):
                    def piece(q):
                        if t is None:
                            return
                        m, p = t
                        if q == 0 and not early(t):
                            pe.wait_ge(S["mean"], done(0, m - 1, p))
                        pe.wait_ge(cnt.made[q], done(0, m, p))
                        if early(t) and p == 0:
                            pe.wait_ge(s_feat[q], 16)
                        for s in range(XB):
                            ins = nc.tensor.matmul(banks[:, p * BANK:p * BANK + 2 * D], cnt.wide[:, q, s, :], feat[:, q * XB + s, :],
                                                   start=(q == 0 and s == 0), stop=(q == PIECES - 1 and s == XB - 1))
                        ins.then_inc(cnt.used[q], 1)

                    for q in range(3):
                        piece(q)
                    if d1 is not None:
                        pe.wait_ge(S["own"], done(0, *d1))
                        for j in range(2):
                            ins = nc.tensor.transpose(banks[:, 2 * BANK + j * P:2 * BANK + (j + 1) * P], both[:, j], ident[:])
                        ins.then_inc(S["turn"], 1)
                    for q in range(3, 6):
                        piece(q)
                    if d1 is not None:
                        if early(d1) and d1[1] == 0:
                            pe.wait_ge(s_wl, 1)
                        pe.wait_ge(S["bh"], done(0, *d1))
                        pe.wait_ge(S["bl"], done(0, *d1))
                        n = 0
                        for j in range(2):
                            for x, part in ((b_h, 0), (b_h, 1), (b_l, 0)):
                                n += 1
                                ins = nc.tensor.matmul(banks[:, 3 * BANK:3 * BANK + D], x[:, j * P:(j + 1) * P], w[:, j, part, :], start=(n == 1), stop=(n == 6))
                        ins.then_inc(S["prod"], 1)
                    piece(6)

                turns(pe, body)

            @block.scalar
            def _(act):
                s = nc.scalar
                credit(act, [cnt.made[q] for q in range(PIECES) if q not in DVE_PIECES])
                credit(act, [S[x] for x in "low bh relu".split()])
                conv = lambda t, q: t is None or cnt.convert(act, lambda d, x: s.activation(d, x, ACT.Copy), 0, t[0], t[1], q)
                for q in range(PIECES):
                    if q not in DVE_PIECES:
                        conv((0, 0), q)
                act.wait_ge(s_wtc, 1)
                s.activation(w[:, :, 0, :], w_t[:], ACT.Copy).then_inc(s_wh, 1)

                def body(t, d1):
                    n = nxt(t) if t is not None else None
                    conv(n, 0)
                    if d1 is not None:
                        m, p = d1
                        act.wait_ge(s_wtc, 1)
                        act.wait_ge(cnt.used[PIECES - 1], done(0, m, p))
                        s.activation(low_sum[:], banks[:, p * BANK + D:p * BANK + 2 * D], ACT.Copy,
                                     scale=deg_inv[:, bass.ds(2 * m + p, 1)]).then_inc(S["low"], 1)
                    conv(n, 2)
                    if d1 is not None:
                        act.wait_ge(S["turn"], done(0, m, p))
                        s.activation(b_h[:], banks[:, 2 * BANK:2 * BANK + 2 * D], ACT.Copy).then_inc(S["bh"], 1)
                    conv(n, 4)
                    if d1 is not None:
                        act.wait_ge(s_wtc, 1)
                        act.wait_ge(S["pre"], done(0, m, p))
                        s.activation(act_h[:, bass.ds(2 * m + p, 1), :].rearrange("p o f -> p (o f)"), pre[:], ACT.Relu).then_inc(S["relu"], 1)
                    conv(n, 6)

                turns(act, body)

            @block.vector
            def _(dve):
                v = nc.vector
                credit(dve, [cnt.made[q] for q in DVE_PIECES])
                credit(dve, [S[x] for x in "mean own bl pre".split()])
                conv = lambda t, q: t is None or cnt.convert(dve, v.tensor_copy, 0, t[0], t[1], q)
                for q in DVE_PIECES:
                    conv((0, 0), q)
                dve.wait_ge(s_wt, 1)
                v.tensor_copy(w_t[:].rearrange("p j f -> p (j f)"), banks[:, 7 * BANK:7 * BANK + 2 * P]).then_inc(s_wtc, 1)
                dve.wait_ge(s_wtc, 1)
                dve.wait_ge(s_wh, 1)
                v.tensor_tensor(w[:, :, 1, :], w_t[:], w[:, :, 0, :].bitcast(F32), ALU.subtract).then_inc(s_wl, 1)
                for q in range(PIECES):
                    dve.wait_ge(s_feat[q], 16)

                def body(t, d1):
                    n = nxt(t) if t is not None else None
                    if d1 is not None:
                        m, p = d1
                        dve.wait_ge(S["low"], done(0, m, p))
                        v.scalar_tensor_tensor(out=both[:, 0], in0=banks[:, p * BANK:p * BANK + D], scalar=deg_inv[:, bass.ds(2 * m + p, 1)],
                                               in1=low_sum[:], op0=ALU.mult, op1=ALU.add).then_inc(S["mean"], 1)
                        x = feat[:, bass.ds(2 * m + p, 1), :].rearrange("p o f -> p (o f)").bitcast(F32)
                        v.tensor_tensor(both[:, 1], x[:, 0:D], x[:, D:], ALU.add).then_inc(S["own"], 1)
                    conv(n, 1)
                    if d1 is not None:
                        dve.wait_ge(S["bh"], done(0, m, p))
                        v.tensor_tensor(b_l[:], banks[:, 2 * BANK:2 * BANK + 2 * D], b_h[:].bitcast(F32), ALU.subtract).then_inc(S["bl"], 1)
                    conv(n, 3)
                    conv(n, 5)
                    if d1 is not None:
                        dve.wait_ge(S["prod"], done(0, m, p))
                        dve.wait_ge(S["relu"], before(0, m, p))
                        v.tensor_tensor(pre[:], banks[:, 3 * BANK:3 * BANK + D], b_row[:], ALU.add).then_inc(S["pre"], 1)

                turns(dve, body)

        with ExitStack() as ctx:
            def sb(name, shape, dt=F32):
                return ctx.enter_context(nc.sbuf_tensor("f_" + name, shape, dt))

            def sem(name):
                return g["sem"]("f_" + name)

            U = 7
            C = T // U
            part_no, real = sb("part_no", [P, 1]), sb("real", [P, 1])
            ones = sb("ones", [P, P])
            gamma, beta = sb("gamma", [P, D]), sb("beta", [P, D])
            sq = sb("sq", [P, T, D])
            f = sb("f", [P, T, D])
            tmp = sb("tmp", [P, 4, D])
            mu, var, scale = sb("mu", [P, D]), sb("var", [P, D]), sb("scale", [P, D])
            half = sb("half", [P, P])
            st, mv, ve, rs = sb("st", [P, T, 6]), sb("mv", [P, T, 2]), sb("ve", [P, T]), sb("rs", [P, T])
            y = sb("y", [P, T, D])
            s_in, s_p, s_mask, s_sum, s_v, s_c, s_sq, s_sqm, s_sum2, s_var, s_scale, s_x2, s_fin, s_st, s_mv, s_ve, s_rs, s_y, s_out = (
                sem(x) for x in ("in part mask sum v centred sq sqm sum2 var scale x2 fin st mv ve rs y out".split()))
            block = ctx.enter_context(nc.Block())
            wide = lambda row, n: row[:].unsqueeze(1).to_broadcast([P, n, D])

            @block.sync
            def _(sp):
                sp.dma_start(gamma[:], broadcast_row(a["L1_gnn_gamma"])).then_inc(s_in, 16)
                sp.dma_start(beta[:], broadcast_row(a["L1_gnn_beta"])).then_inc(s_in, 16)
                for c in range(C):
                    sp.wait_ge(s_y, c + 1)
                    n = U if c < C - 1 else U - 1
                    sp.dma_start(out[c * U * P:(c * U + n) * P, :].rearrange("(t p) d -> p t d", p=P), y[:, c * U:c * U + n, :]).then_inc(s_out, 16)
                sp.dma_start(out[(T - 1) * P:N, :], y[0:LAST, T - 1, :]).then_inc(s_out, 16)
                sp.wait_ge(s_out, 16 * (C + 1))

            @block.tensor
            def _(pe):
                def total(src, at, s, needs):
                    n = -(-T // 4)
                    for j in range(n):
                        w_ = min(4, T - 4 * j)
                        needs(4 * j + w_)
                        ins = nc.tensor.matmul(banks[:, at:at + w_ * D], ones[:], src[:, 4 * j:4 * j + w_, :].rearrange("p t d -> p (t d)"),
                                               start=(j == 0), stop=(j == n - 1), skip_group_check=True)
                    ins.then_inc(s, 1)

                pe.wait_ge(s_mask, 1)
                total(act_h, 0, s_sum, lambda t: None)

                def squared(t):
                    pe.wait_ge(s_sq, min(C, -(-t // U)))
                    if t == T:
                        pe.wait_ge(s_sqm, 1)

                total(sq, BANK, s_sum2, squared)

            @block.gpsimd
            def _(pool):
                gp = nc.gpsimd
                gp.iota(part_no[:], [[0, 1]], base=0, channel_multiplier=1, allow_small_or_imprecise_dtypes=True).then_inc(s_p, 1)
                gp.memset(half[:], -0.5).then_inc(s_p, 1)
                pool.wait_ge(s_var, 1)
                pool.wait_ge(s_p, 2)
                gp.tensor_tensor(scale[:], var[:], half[:], ALU.pow).then_inc(s_scale, 1)
                for c in range(C):
                    pool.wait_ge(s_mv, c + 1)
                    gp.tensor_scalar(ve[:, c * U:(c + 1) * U], mv[:, c * U:(c + 1) * U, 1], EPS, None, ALU.add).then_inc(s_ve, 1)
                    pool.wait_ge(s_ve, c + 1)
                    gp.tensor_tensor(rs[:, c * U:(c + 1) * U], ve[:, c * U:(c + 1) * U], half[:, 0:U], ALU.pow).then_inc(s_rs, 1)

            @block.scalar
            def _(act):
                for c in range(C):
                    act.wait_ge(s_c, c + 1)
                    nc.scalar.activation(sq[:, c * U:(c + 1) * U], f[:, c * U:(c + 1) * U], ACT.Square).then_inc(s_sq, 1)

            @block.vector
            def _(dve):
                v = nc.vector
                n = [0]

                def link(ins):
                    n[0] += 1
                    ins.then_inc(s_v, 1)
                    dve.wait_ge(s_v, n[0])

                v.memset(ones[:], 1.0)
                dve.wait_ge(s_p, 1)
                link(v.tensor_scalar(real[:], part_no[:], float(LAST), None, ALU.is_lt))
                v.tensor_scalar(act_h[:, T - 1], act_h[:, T - 1], real[:, 0:1], None, ALU.mult).then_inc(s_mask, 1)

                def mean(at, to, s):
                    dve.wait_ge(s, 1)
                    link(v.tensor_copy(tmp[:].rearrange("p t d -> p (t d)"), banks[:, at:at + 4 * D]))
                    link(v.tensor_tensor(tmp[:, 0:2], tmp[:, 0:2], tmp[:, 2:4], ALU.add))
                    link(v.tensor_tensor(to[:], tmp[:, 0], tmp[:, 1], ALU.add))

                mean(0, mu, s_sum)
                link(v.tensor_scalar(mu[:], mu[:], 1.0 / N, None, ALU.mult))
                dve.wait_ge(s_mask, 1)
                for c in range(C):
                    v.tensor_tensor(f[:, c * U:(c + 1) * U], act_h[:, c * U:(c + 1) * U], wide(mu, U), ALU.subtract).then_inc(s_c, 1)
                dve.wait_ge(s_sq, C)
                v.tensor_scalar(sq[:, T - 1], sq[:, T - 1], real[:, 0:1], None, ALU.mult).then_inc(s_sqm, 1)
                mean(BANK, var, s_sum2)
                v.tensor_scalar(var[:], var[:], 1.0 / N, EPS, ALU.mult, ALU.add).then_inc(s_var, 1)
                dve.wait_ge(s_in, 32)
                x = feat[:].bitcast(F32)
                link(v.tensor_tensor(y[:], x[:, :, 0:D], x[:, :, D:], ALU.add))
                link(v.scalar_tensor_tensor(out=y[:], in0=y[:], scalar=2.0, in1=wide(beta, T), op0=ALU.mult, op1=ALU.add))
                dve.wait_ge(s_scale, 1)
                link(v.tensor_tensor(scale[:], scale[:], gamma[:], ALU.mult))
                dve.wait_ge(s_c, C)
                for c in range(C):
                    part = slice(c * U, (c + 1) * U)
                    link(v.tensor_tensor(f[:, part], f[:, part], wide(scale, U), ALU.mult))
                    link(v.tensor_tensor(f[:, part], f[:, part], y[:, part], ALU.add))
                    for t in range(c * U, (c + 1) * U):
                        ins = v.bn_stats(st[:, t], f[:, t])
                    ins.then_inc(s_st, 1)
                    dve.wait_ge(s_st, c + 1)
                    for t in range(c * U, (c + 1) * U):
                        ins = v.bn_aggr(mv[:, t], st[:, t])
                    ins.then_inc(s_mv, 1)
                    dve.wait_ge(s_mv, c + 1)
                    dve.wait_ge(s_rs, c + 1)
                    for t in range(c * U, (c + 1) * U):
                        ins = v.tensor_scalar(y[:, t], f[:, t], mv[:, t, 0:1], rs[:, t:t + 1], ALU.subtract, ALU.mult)
                    ins.then_inc(s_y, 1)


def kernel(**inputs):
    import numpy as np
    import concourse.bacc as bacc
    from concourse.bass_utils import run_bass_kernel_spmd

    nc = bacc.Bacc("TRN2", target_bir_lowering=False, num_devices=1)
    arrays = {name: np.ascontiguousarray(v) for name, v in inputs.items()}
    a = {name: nc.dram_tensor(name, v.shape, mybir.dt.from_np(v.dtype), kind="ExternalInput").ap() for name, v in arrays.items()}
    out = nc.dram_tensor("out", tuple(arrays["x"].shape), F32, kind="ExternalOutput").ap()
    gnn_kernel(nc, a, out)
    r = run_bass_kernel_spmd(nc, [arrays], core_ids=[0])
    return r.results[0]["out"]
```
